# Optimizing a Trainium2 kernel written in Bass

```python
import numpy as np
import jax
import jax.numpy as jnp

def _softmax(x, axis=-1):
    return jax.nn.softmax(x, axis=axis)

def _gelu(x):
    return jax.nn.gelu(x, approximate=True)

def _silu(x):
    return jax.nn.silu(x)

def _sigmoid(x):
    return jax.nn.sigmoid(x)

def _layernorm(x, axis=-1, eps=1e-05):
    m = jnp.mean(x, axis=axis, keepdims=True)
    v = jnp.var(x, axis=axis, keepdims=True)
    return (x - m) / jnp.sqrt(v + eps)

def _scatter_add(tgt, idx, src, axis=0):
    return tgt.at[idx].add(src)

def _segment_sum(src, seg, n):
    return jax.ops.segment_sum(src, seg, n)
kernel_name = 'mk_adj_resnorm_d1_adj_r2_c9d2d6'

def setup_inputs(seed: int=0):
    np.random.seed(seed)
    _w = jnp.asarray

    def _rec_inputs():
        import jax
        import jax.numpy as jnp
        _gk = jax.random.key(seed)
        x = -0.000929 + 1 * jax.random.normal(jax.random.fold_in(_gk, 1), (8, 2048, 64), jnp.float32)
        _a = jax.random.bernoulli(jax.random.fold_in(_gk, 2), 0.00390625, (8, 2048, 2048))
        _a = jnp.logical_or(_a, jnp.swapaxes(_a, -1, -2))
        _a = jnp.logical_or(_a, jnp.eye(2048, dtype=bool))
        _af = _a.astype(jnp.float32)
        _af = _af * jax.random.uniform(jax.random.fold_in(_gk, 3), (8, 2048, 2048), jnp.float32, 0.05, 1)
        adj = _af
        return (x, adj)
    x, adj = _rec_inputs()

    def _L0_gnn_setup():
        import jax, jax.numpy as jnp
        import numpy as np
        B, N, C, R = (4, 2048, 64, 16)
        EPS = 1e-12
        key = jax.random.key(seed)
        k_x, k_w, k_u = jax.random.split(key, 3)
        x = jax.random.normal(k_x, (B, N, C), dtype=jnp.float32)
        W = jax.random.uniform(k_w, (B, N, N), dtype=jnp.float32)
        U = 0.01 * jax.random.normal(k_u, (N, R), dtype=jnp.float32)
        w_scale = jnp.asarray(1.0, dtype=jnp.float32)
        return {'x': x, 'W': W, 'U': U, 'w_scale': w_scale}
    _L0_gnn_all = _L0_gnn_setup()
    _L0_gnn_in = {k: v for k, v in _L0_gnn_all.items() if k in ('U', 'w_scale')}
    del _L0_gnn_all
    return {'x': x, 'adj': adj, 'L0_gnn_U': _L0_gnn_in['U'], 'L0_gnn_w_scale': _L0_gnn_in['w_scale']}

def reference(x, adj, L0_gnn_U, L0_gnn_w_scale):
    import jax
    import jax.numpy as jnp

    def _L0_gnn_ref(x, W, U, w_scale):
        import jax, jax.numpy as jnp
        import numpy as np
        B, N, C, R = (4, 2048, 64, 16)
        EPS = 1e-12
        Ws = 0.5 * (W + jnp.swapaxes(W, -1, -2))
        A = jax.nn.sigmoid(U @ U.T)
        K = Ws * A[None, :, :]
        deg = jnp.maximum(K.sum(axis=-1), EPS)
        d = jax.lax.rsqrt(deg)
        K = K * d[:, :, None] * d[:, None, :]
        return w_scale * jnp.einsum('bnm,bmc->bnc', K, x)
    x = _layernorm(x + _L0_gnn_ref(x, adj, L0_gnn_U, L0_gnn_w_scale), axis=-1)
    return x

_drawn_inputs = setup_inputs


def setup_inputs(seed=0):
    import zlib

    import numpy as np

    out = dict(_drawn_inputs(seed))
    spreads = {}
    factors = {'L0_gnn_U': 64.0}
    for name, (base, spread) in spreads.items():
        noise = np.random.default_rng([zlib.crc32(name.encode()), seed]).standard_normal(out[name].shape)
        drawn = base * np.exp(spread * noise) if base else spread * noise
        out[name] = jnp.asarray(drawn.astype(out[name].dtype))
    for name, factor in factors.items():
        out[name] = (out[name] * factor).astype(out[name].dtype)
    return out
```

```python
import concourse.bass as bass
from concourse import mybir
from contextlib import ExitStack


def graph_conv_norm(nc: bass.Bass, x: bass.AP, adj: bass.AP, U: bass.AP, w_scale: bass.AP, out: bass.AP):
    fp32 = mybir.dt.float32
    ALU = mybir.AluOpType
    ACT = mybir.ActivationFunctionType
    AX = mybir.AxisListType

    B, N, C = x.shape
    R = U.shape[1]
    P = 128
    NT = N // P
    S = 4
    SQ = S * P
    HALF = SQ // 2
    EPS_DEG = 1e-12
    EPS_LN = 1e-5

    STEPS = [(I, J) for I in range(S) for J in range(I, S)]
    NS = len(STEPS)
    LAG = 3
    SLOTS = NS + LAG + 1
    NORM_SLOT = NS
    SUMS = S * NS
    BANDS = {s: list(range(1 if I == J else 0, S)) for s, (I, J) in enumerate(STEPS)}
    MIRRORS = sum(len(v) for v in BANDS.values())
    MIRROR_AT = {}
    for s in range(NS):
        for c in BANDS[s]:
            MIRROR_AT[s, c] = len(MIRROR_AT)

    A_AT, a_cols = {}, 0
    for s, (I, J) in enumerate(STEPS):
        for r in range(S):
            A_AT[s, r] = a_cols
            a_cols += SQ - r * P if I == J else SQ

    adj_v = adj.rearrange("b (i r p) m -> b i p r m", r=S, p=P)
    x_v = x.rearrange("b (t p) c -> b p t c", p=P)
    out_v = out.rearrange("b (t p) c -> b p t c", p=P)
    U_v = U.rearrange("(t p) r -> p t r", p=P)

    ctx = ExitStack()
    with ctx:
        def sb(name, shape):
            return ctx.enter_context(nc.sbuf_tensor(name, shape, fp32))

        def sem(name):
            return ctx.enter_context(nc.semaphore(name))

        K = sb("K", [P, S, S, S, SQ])
        A = sb("A", [P, a_cols])
        work = sb("work", [P, 2 * NT * C])
        xs = work[:, 0:NT * C].rearrange("p (t c) -> p t c", c=C)
        yT = work[:, 0:NT * C]
        z = work[:, NT * C:2 * NT * C].rearrange("p (t c) -> p t c", c=C)
        UT = work[0:R, 0:N]
        Un = K[:, S - 1, S - 1, 0, 0:NT * R].rearrange("p (t r) -> p t r", r=R)
        ident = sb("ident", [P, P])
        part = sb("part", [P, NT, S + 1])
        deg2 = sb("deg2", [P, NT])
        deg = sb("deg", [P, NT])
        root = sb("root", [P, NT])
        inv = sb("inv", [P, NT])
        nwt = sb("nwt", [P, NT])
        d = sb("d", [P, NT])
        dw = sb("dw", [P, NT])
        wsc = sb("wsc", [P, 1])
        wsh = sb("wsh", [P, 1])
        zsum = sb("zsum", [P, NT])
        nmean = sb("nmean", [P, NT])
        zsq = sb("zsq", [P, NT])
        var = sb("var", [P, NT])
        rstd = sb("rstd", [P, NT])

        acc = ctx.enter_context(nc.psum_tensor("acc", [P, S * HALF], fp32))
        psT = ctx.enter_context(nc.psum_tensor("psT", [P, 2, SQ], fp32))
        psM = ctx.enter_context(nc.psum_tensor("psM", [P, 2, SQ], fp32))
        psY = ctx.enter_context(nc.psum_tensor("psY", [P, NT * C], fp32))

        w_in = [[sem(f"w_in_{I}{J}") for J in range(S)] for I in range(S)]
        u_in = sem("u_in")
        s_in = sem("s_in")
        x_in = sem("x_in")
        r_in = sem("r_in")
        out_done = sem("out_done")
        zeros = sem("zeros")
        ident_ready = sem("ident_ready")
        part_zero = sem("part_zero")
        ut_ready = sem("ut_ready")
        ut_copied = sem("ut_copied")
        uu_ready = sem("uu_ready")
        a_ready = sem("a_ready")
        wt_ready = sem("wt_ready")
        sum_done = sem("sum_done")
        k_up = sem("k_up")
        kt_ready = sem("kt_ready")
        k_low = sem("k_low")
        deg_step = sem("deg_step")
        deg_ready = sem("deg_ready")
        root_ready = sem("root_ready")
        xs_ready = sem("xs_ready")
        dw_ready = sem("dw_ready")
        product_done = sem("product_done")
        yT_ready = sem("yT_ready")
        y_ready = sem("y_ready")
        z_ready = sem("z_ready")
        nmean_ready = sem("nmean_ready")
        centred = sem("centred")
        zsq_ready = sem("zsq_ready")
        var_ready = sem("var_ready")
        std_ready = sem("std_ready")
        ln_step = sem("ln_step")
        rstd_ready = sem("rstd_ready")
        norm_done = sem("norm_done")

        block = ctx.enter_context(nc.Block())

        @block.sync
        def _(sp):
            def load(b, s):
                I, J = STEPS[s]
                for r, c in ((J, I), (I, J))[:1 if I == J else 2]:
                    sp.dma_start(K[:, r, c, :, :], adj_v[b, r, :, :, c * SQ:(c + 1) * SQ]).then_inc(w_in[r][c], 16)

            sp.dma_start(Un, U_v).then_inc(u_in, 16)
            sp.dma_start(wsc[:, :], w_scale.partition_broadcast(P)).then_inc(s_in, 16)
            for s in range(NS - 1):
                load(0, s)
            sp.wait_ge(ut_ready, 1)
            load(0, NS - 1)
            sp.wait_ge(uu_ready, SUMS)
            sp.dma_start(xs, x_v[0]).then_inc(x_in, 16)
            with sp.Fori(1, B) as b:
                for s in range(NS):
                    sp.wait_ge(product_done, (b - 1) * NS + s + 1)
                    load(b, s)
                sp.wait_ge(y_ready, b)
                sp.dma_start(xs, x_v[b]).then_inc(x_in, 16)

        @block.tensor
        def _(pe):
            def outer(s):
                I, J = STEPS[s]
                for r in range(S):
                    g = s * S + r
                    c0 = r * P if I == J else 0
                    if g >= 2:
                        pe.wait_ge(a_ready, g - 1)
                    i = I * S + r
                    nc.tensor.matmul(psY[:, (g % 2) * SQ:(g % 2) * SQ + SQ - c0], UT[:, i * P:(i + 1) * P],
                                     UT[:, J * SQ + c0:(J + 1) * SQ], start=True, stop=True).then_inc(uu_ready, 1)

            def transpose_w(b, s, first):
                I, J = STEPS[s]
                pe.wait_ge(w_in[J][I], 16 * (b + 1))
                for r in range(S):
                    g = s * S + r
                    if not first or g >= 2:
                        pe.wait_ge(sum_done, b * SUMS + g - 1)
                    for c in range(r if I == J else 0, S):
                        last = nc.tensor.transpose(psT[:, g % 2, c * P:(c + 1) * P],
                                                   K[:, J, I, c, r * P:(r + 1) * P], ident[:, :])
                    last.then_inc(wt_ready, 1)

            def transpose_k(b, s, first):
                I, J = STEPS[s]
                pe.wait_ge(k_up, b * SUMS + (s + 1) * S)
                for c in BANDS[s]:
                    g = MIRROR_AT[s, c]
                    if not first or g >= 2:
                        pe.wait_ge(k_low, b * MIRRORS + g - 1)
                    for r in range(c if I == J else S):
                        last = nc.tensor.transpose(psM[:, g % 2, r * P:(r + 1) * P],
                                                   K[:, I, J, r, c * P:(c + 1) * P], ident[:, :])
                    last.then_inc(kt_ready, 1)

            def product(b, s):
                I, J = STEPS[s]
                pe.wait_ge(xs_ready, b * S + J + 1)
                for rows, cols in ((I, J), (J, I))[:1 if I == J else 2]:
                    for r in range(S):
                        for h in range(2):
                            moving = K[:, rows, cols, r, :].rearrange("p (k h q) -> p k h q", h=2, q=P)[:, :, h, :]
                            into = acc[h * C:(h + 1) * C, cols * HALF:(cols + 1) * HALF]
                            last = nc.tensor.matmul(into.rearrange("p (k q) -> p k q", q=P), xs[:, rows * S + r, :],
                                                    moving, start=(s in (0, 2) and rows == 0 and r == 0),
                                                    stop=(s == NS - 1 and r == S - 1), skip_group_check=True)
                last.then_inc(product_done, 1)

            def transpose_y(b):
                pe.wait_ge(yT_ready, 2 * (b + 1))
                for q in range(NT // 2):
                    last = nc.tensor.transpose(psY[:, q * P:(q + 1) * P], yT[:, q * P:(q + 1) * P], ident[:, :])
                last.then_inc(y_ready, 1)

            pe.wait_ge(u_in, 16)
            pe.wait_ge(ident_ready, 1)
            for t in range(NT):
                into = psY if t < NT // 2 else acc
                t0 = t % (NT // 2) * P
                last = nc.tensor.transpose(into[0:R, t0:t0 + P], Un[:, t, :], ident[:, :])
            last.then_inc(ut_ready, 1)
            pe.wait_ge(ut_copied, 2)
            for k in range(NS + 1):
                if k < NS:
                    outer(k)
                    transpose_w(0, k, True)
                if k >= 1:
                    transpose_k(0, k - 1, True)
            with pe.Fori(1, B) as b:
                for k in range(SLOTS):
                    if k < NS:
                        product(b - 1, k)
                    if 0 <= k - LAG < NS:
                        transpose_w(b, k - LAG, False)
                    if 0 <= k - LAG - 1:
                        transpose_k(b, k - LAG - 1, False)
                    if k == NORM_SLOT:
                        transpose_y(b - 1)
            for s in range(NS):
                product(B - 1, s)
            transpose_y(B - 1)

        @block.vector
        def _(dve):
            def sum_row(b, s, r):
                I, J = STEPS[s]
                g, c0 = s * S + r, r * P if I == J else 0
                if r == 0:
                    dve.wait_ge(w_in[I][J], 16 * (b + 1))
                dve.wait_ge(wt_ready, b * SUMS + g + 1)
                row = K[:, I, J, r, c0:SQ]
                nc.vector.tensor_tensor(row, psT[:, g % 2, c0:SQ], row, ALU.add).then_inc(sum_done, 1)

            def times_a(b, s, r, first):
                I, J = STEPS[s]
                g, c0 = s * S + r, r * P if I == J else 0
                dve.wait_ge(sum_done, b * SUMS + g + 1)
                if first:
                    dve.wait_ge(a_ready, g + 1)
                row = K[:, I, J, r, c0:SQ]
                nc.vector.scalar_tensor_tensor(row, row, 1.0, A[:, A_AT[s, r]:A_AT[s, r] + SQ - c0], ALU.mult, ALU.mult,
                                               accum_out=part[:, I * S + r, J:J + 1]).then_inc(k_up, 1)

            def build(b, s, first):
                for r in range(S):
                    sum_row(b, s, r)
                    if r:
                        times_a(b, s, r - 1, first)
                    elif s:
                        times_a(b, s - 1, S - 1, first)
                if s == NS - 1:
                    times_a(b, s, S - 1, first)

            def rsqrt(square, root_in, to, done, step, at):
                nc.vector.reciprocal(inv[:, :], root_in).then_inc(step, 1)
                dve.wait_ge(step, at + 1)
                nc.vector.tensor_tensor(nwt[:, :], inv[:, :], inv[:, :], ALU.mult).then_inc(step, 1)
                dve.wait_ge(step, at + 2)
                nc.vector.scalar_tensor_tensor(nwt[:, :], nwt[:, :], -0.5, square, ALU.mult, ALU.mult).then_inc(step, 1)
                dve.wait_ge(step, at + 3)
                nc.vector.scalar_tensor_tensor(to, nwt[:, :], 1.5, inv[:, :], ALU.add, ALU.mult).then_inc(done, 1)

            def scale_x(b):
                dve.wait_ge(k_up, (b + 1) * SUMS)
                dve.wait_ge(k_low, (b + 1) * MIRRORS)
                nc.vector.reduce_sum(deg2[:, :], part[:, :, :], AX.X).then_inc(deg_step, 1)
                dve.wait_ge(deg_step, 5 * b + 1)
                nc.vector.tensor_scalar(deg[:, :], deg2[:, :], 0.5, EPS_DEG, ALU.mult, ALU.max).then_inc(deg_ready, 1)
                dve.wait_ge(root_ready, b + 1)
                rsqrt(deg[:, :], root[:, :], d[:, :], deg_step, deg_step, 5 * b + 1)
                dve.wait_ge(deg_step, 5 * b + 5)
                dve.wait_ge(x_in, 16 * (b + 1))
                for I in range(S):
                    rows = xs[:, I * S:(I + 1) * S, :]
                    nc.vector.tensor_tensor(rows, rows, d[:, I * S:(I + 1) * S].unsqueeze(2).to_broadcast([P, S, C]),
                                            ALU.mult).then_inc(xs_ready, 1)
                nc.vector.tensor_scalar(dw[:, :], d[:, :], wsh[:, 0:1], None, ALU.mult).then_inc(dw_ready, 1)

            def residual(b):
                dve.wait_ge(y_ready, b + 1)
                dve.wait_ge(r_in, 16 * (b + 1))
                dve.wait_ge(dw_ready, b + 1)
                for t in range(NT):
                    last = nc.vector.scalar_tensor_tensor(z[:, t, :], psY[:, t * C:(t + 1) * C], dw[:, t:t + 1],
                                                          z[:, t, :], ALU.mult, ALU.add, accum_out=zsum[:, t:t + 1])
                last.then_inc(z_ready, 1)
                dve.wait_ge(z_ready, b + 1)
                nc.vector.tensor_scalar(nmean[:, :], zsum[:, :], -1.0 / C, None, ALU.mult).then_inc(nmean_ready, 1)

            def deviation(b):
                dve.wait_ge(zsq_ready, b + 1)
                nc.vector.tensor_scalar(var[:, :], zsq[:, :], 1.0 / C, EPS_LN, ALU.mult, ALU.add).then_inc(var_ready, 1)
                dve.wait_ge(std_ready, b + 1)
                rsqrt(var[:, :], zsum[:, :], rstd[:, :], rstd_ready, ln_step, 3 * b)

            nc.vector.memset(part[:, :, S:S + 1], 0.0).then_inc(part_zero, 1)
            dve.wait_ge(s_in, 16)
            nc.vector.tensor_scalar(wsh[:, :], wsc[:, :], 0.5, None, ALU.mult)
            dve.wait_ge(ut_ready, 1)
            for h, src in enumerate((psY, acc)):
                nc.vector.tensor_copy(UT[:, h * N // 2:(h + 1) * N // 2], src[0:R, :]).then_inc(ut_copied, 1)
            for s in range(NS):
                build(0, s, True)
            scale_x(0)
            with dve.Fori(1, B) as b:
                for k in range(LAG, SLOTS - 1):
                    build(b, k - LAG, False)
                    if k == NORM_SLOT:
                        residual(b - 1)
                scale_x(b)
                deviation(b - 1)
            residual(B - 1)
            deviation(B - 1)

        @block.scalar
        def _(act):
            def sigmoid(s):
                I, J = STEPS[s]
                for r in range(S):
                    g, n = s * S + r, SQ - r * P if I == J else SQ
                    act.wait_ge(uu_ready, g + 1)
                    nc.scalar.activation(A[:, A_AT[s, r]:A_AT[s, r] + n], psY[:, (g % 2) * SQ:(g % 2) * SQ + n],
                                         ACT.Sigmoid).then_inc(a_ready, 1)

            def mirror(b, s):
                I, J = STEPS[s]
                for c in BANDS[s]:
                    g, n = MIRROR_AT[s, c], c * P if I == J else SQ
                    act.wait_ge(kt_ready, b * MIRRORS + g + 1)
                    at = S if I == J else I
                    nc.scalar.activation(K[:, J, I, c, 0:n], psM[:, g % 2, 0:n], ACT.Copy,
                                         accum_out=part[:, J * S + c, at:at + 1]).then_inc(k_low, 1)

            def drain_y(b):
                act.wait_ge(product_done, (b + 1) * NS)
                for h in range(2):
                    nc.scalar.copy(yT[:, h * SQ:(h + 1) * SQ], acc[:, h * SQ:(h + 1) * SQ]).then_inc(yT_ready, 1)

            def squares(b):
                act.wait_ge(centred, b + 1)
                for t in range(NT):
                    last = nc.scalar.activation(psY[:, t * C:(t + 1) * C], z[:, t, :], ACT.Square,
                                                accum_out=zsq[:, t:t + 1])
                last.then_inc(zsq_ready, 1)

            def root_of_deg(b):
                act.wait_ge(deg_ready, b + 1)
                nc.scalar.activation(root[:, :], deg[:, :], ACT.Sqrt).then_inc(root_ready, 1)

            def root_of_var(b):
                act.wait_ge(var_ready, b + 1)
                nc.scalar.activation(zsum[:, :], var[:, :], ACT.Sqrt).then_inc(std_ready, 1)

            for k in range(NS + 1):
                if k < NS:
                    sigmoid(k)
                if k == 1:
                    act.wait_ge(part_zero, 1)
                if k >= 1:
                    mirror(0, k - 1)
            root_of_deg(0)
            with act.Fori(1, B) as b:
                for k in range(LAG + 1, SLOTS):
                    if k == NORM_SLOT:
                        drain_y(b - 1)
                    mirror(b, k - LAG - 1)
                    if k == SLOTS - 2:
                        squares(b - 1)
                root_of_deg(b)
                root_of_var(b - 1)
            drain_y(B - 1)
            squares(B - 1)
            root_of_var(B - 1)

        @block.gpsimd
        def _(pool):
            def normalise(b):
                pool.wait_ge(z_ready, b + 1)
                pool.wait_ge(nmean_ready, b + 1)
                nc.gpsimd.tensor_tensor(z, z, nmean[:, :].unsqueeze(2).to_broadcast([P, NT, C]),
                                        ALU.add).then_inc(centred, 1)
                pool.wait_ge(centred, b + 1)
                pool.wait_ge(zsq_ready, b + 1)
                pool.wait_ge(rstd_ready, b + 1)
                nc.gpsimd.tensor_tensor(z, z, rstd[:, :].unsqueeze(2).to_broadcast([P, NT, C]),
                                        ALU.mult).then_inc(norm_done, 1)
                pool.wait_ge(norm_done, b + 1)
                pool.dma_start(out_v[b], z).then_inc(out_done, 16)

            nc.gpsimd.memset(ident[:, :], 0.0).then_inc(zeros, 1)
            pool.wait_ge(zeros, 1)
            nc.gpsimd.affine_select(out=ident[:, :], in_=ident[:, :], compare_op=ALU.not_equal, fill=1.0, base=0,
                                    pattern=[[-1, P]], channel_multiplier=1).then_inc(ident_ready, 1)
            pool.wait_ge(uu_ready, SUMS)
            pool.dma_start(z, x_v[0]).then_inc(r_in, 16)
            with pool.Fori(1, B) as b:
                normalise(b - 1)
                pool.wait_ge(out_done, 16 * b)
                pool.dma_start(z, x_v[b]).then_inc(r_in, 16)
            normalise(B - 1)
            pool.wait_ge(out_done, 16 * B)


_INS = ["x", "adj", "L0_gnn_U", "L0_gnn_w_scale"]
_OUT = ((8, 2048, 64), "float32")


def kernel(**inputs):
    import numpy as _np
    import concourse.bacc as _bacc
    from concourse import mybir as _mybir
    from concourse.bass_utils import run_bass_kernel_spmd as _run

    nc = _bacc.Bacc("TRN2", target_bir_lowering=False, num_devices=1)
    arrays, args = {}, []
    for name in _INS:
        a = _np.ascontiguousarray(inputs[name])
        arrays[f"in_{name}_dram"] = a
        args.append(nc.dram_tensor(f"in_{name}_dram", a.shape, _mybir.dt.from_np(a.dtype), kind="ExternalInput").ap())
    shape, dtype = _OUT
    args.append(nc.dram_tensor("out_dram", shape, _mybir.dt.from_np(_np.dtype(dtype)), kind="ExternalOutput").ap())
    graph_conv_norm(nc, *args)
    r = _run(nc, [arrays], core_ids=[0])
    return r.results[0]["out_dram"]
```

```python
import concourse.bass as bass
from concourse import mybir
from contextlib import ExitStack


def graph_conv_norm(nc: bass.Bass, x: bass.AP, adj: bass.AP, U: bass.AP, w_scale: bass.AP, out: bass.AP):
    fp32 = mybir.dt.float32
    ALU = mybir.AluOpType
    ACT = mybir.ActivationFunctionType
    AX = mybir.AxisListType

    B, N, C = x.shape
    R = U.shape[1]
    P = 128
    NT = N // P
    S = 4
    SQ = S * P
    HALF = SQ // 2
    EPS_DEG = 1e-12
    EPS_LN = 1e-5

    STEPS = [(I, J) for I in range(S) for J in range(I, S)]
    NS = len(STEPS)
    ROWS = [(s, r) for s in range(NS) for r in range(S)]
    SUMS = len(ROWS)
    MIRROR_AT = {}
    for s, r in ROWS:
        if r or STEPS[s][0] != STEPS[s][1]:
            MIRROR_AT[s, r] = len(MIRROR_AT)
    MIRRORS = len(MIRROR_AT)
    LAG = 10
    LAG_K = 6
    BEATS = SUMS + LAG + LAG_K

    def at_beat(t, lag):
        return ROWS[t - lag] if 0 <= t - lag < SUMS else None

    A_AT, a_cols = {}, 0
    for s, (I, J) in enumerate(STEPS):
        for r in range(S):
            A_AT[s, r] = a_cols
            a_cols += SQ - r * P if I == J else SQ

    adj_v = adj.rearrange("b (i r p) m -> b i p r m", r=S, p=P)
    x_v = x.rearrange("b (t p) c -> b p t c", p=P)
    out_v = out.rearrange("b (t p) c -> b p t c", p=P)
    U_v = U.rearrange("(t p) r -> p t r", p=P)

    ctx = ExitStack()
    with ctx:
        def sb(name, shape):
            return ctx.enter_context(nc.sbuf_tensor(name, shape, fp32))

        def sem(name):
            return ctx.enter_context(nc.semaphore(name))

        K = sb("K", [P, S, S, S, SQ])
        A = sb("A", [P, a_cols])
        work = sb("work", [P, 2 * NT * C])
        xs = work[:, 0:NT * C].rearrange("p (t c) -> p t c", c=C)
        yT = work[:, 0:NT * C]
        z = work[:, NT * C:2 * NT * C].rearrange("p (t c) -> p t c", c=C)
        UT = work[0:R, 0:N]
        Un = K[:, S - 1, S - 1, 0, 0:NT * R].rearrange("p (t r) -> p t r", r=R)
        ident = sb("ident", [P, P])
        part = sb("part", [P, NT, S + 1])
        deg2 = sb("deg2", [P, NT])
        deg = sb("deg", [P, NT])
        root = sb("root", [P, NT])
        inv = sb("inv", [P, NT])
        nwt = sb("nwt", [P, NT])
        d = sb("d", [P, NT])
        dw = sb("dw", [P, NT])
        wsc = sb("wsc", [P, 1])
        wsh = sb("wsh", [P, 1])
        zsum = sb("zsum", [P, NT])
        nmean = sb("nmean", [P, NT])
        zsq = sb("zsq", [P, NT])
        var = sb("var", [P, NT])
        rstd = sb("rstd", [P, NT])

        acc = ctx.enter_context(nc.psum_tensor("acc", [P, S * HALF], fp32))
        psT = ctx.enter_context(nc.psum_tensor("psT", [P, 2, SQ], fp32))
        psM = ctx.enter_context(nc.psum_tensor("psM", [P, 2, SQ], fp32))
        psY = ctx.enter_context(nc.psum_tensor("psY", [P, NT * C], fp32))

        w_in = [[sem(f"w_in_{I}{J}") for J in range(S)] for I in range(S)]
        u_in = sem("u_in")
        s_in = sem("s_in")
        x_in = sem("x_in")
        r_in = sem("r_in")
        out_done = sem("out_done")
        zeros = sem("zeros")
        ident_ready = sem("ident_ready")
        part_zero = sem("part_zero")
        ut_ready = sem("ut_ready")
        ut_copied = sem("ut_copied")
        uu_ready = sem("uu_ready")
        a_ready = sem("a_ready")
        wt_ready = sem("wt_ready")
        sum_done = sem("sum_done")
        k_up = sem("k_up")
        kt_ready = sem("kt_ready")
        k_low = sem("k_low")
        deg_step = sem("deg_step")
        deg_ready = sem("deg_ready")
        root_ready = sem("root_ready")
        xs_ready = sem("xs_ready")
        dw_ready = sem("dw_ready")
        product_done = sem("product_done")
        yT_ready = sem("yT_ready")
        y_ready = sem("y_ready")
        z_ready = sem("z_ready")
        nmean_ready = sem("nmean_ready")
        centred = sem("centred")
        zsq_ready = sem("zsq_ready")
        var_ready = sem("var_ready")
        std_ready = sem("std_ready")
        ln_step = sem("ln_step")
        rstd_ready = sem("rstd_ready")
        norm_done = sem("norm_done")

        block = ctx.enter_context(nc.Block())

        @block.sync
        def _(sp):
            def load(b, s):
                I, J = STEPS[s]
                for r, c in ((J, I), (I, J))[:1 if I == J else 2]:
                    sp.dma_start(K[:, r, c, :, :], adj_v[b, r, :, :, c * SQ:(c + 1) * SQ]).then_inc(w_in[r][c], 16)

            sp.dma_start(Un, U_v).then_inc(u_in, 16)
            sp.dma_start(wsc[:, :], w_scale.partition_broadcast(P)).then_inc(s_in, 16)
            for s in range(NS - 1):
                load(0, s)
            sp.wait_ge(ut_ready, 1)
            load(0, NS - 1)
            sp.wait_ge(uu_ready, SUMS)
            sp.dma_start(xs, x_v[0]).then_inc(x_in, 16)
            with sp.Fori(1, B) as b:
                for s in range(NS):
                    sp.wait_ge(product_done, (b - 1) * NS + s + 1)
                    load(b, s)
                sp.wait_ge(y_ready, b)
                sp.dma_start(xs, x_v[b]).then_inc(x_in, 16)

        @block.tensor
        def _(pe):
            def outer(s, r):
                I, J = STEPS[s]
                g, i, c0 = s * S + r, I * S + r, r * P if I == J else 0
                if g >= 2:
                    pe.wait_ge(a_ready, g - 1)
                nc.tensor.matmul(psY[:, (g % 2) * SQ:(g % 2) * SQ + SQ - c0], UT[:, i * P:(i + 1) * P],
                                 UT[:, J * SQ + c0:(J + 1) * SQ], start=True, stop=True).then_inc(uu_ready, 1)

            def transpose_w(b, s, r, first):
                I, J = STEPS[s]
                g = s * S + r
                if r == 0:
                    pe.wait_ge(w_in[J][I], 16 * (b + 1))
                if not first or g >= 2:
                    pe.wait_ge(sum_done, b * SUMS + g - 1)
                for c in range(r if I == J else 0, S):
                    last = nc.tensor.transpose(psT[:, g % 2, c * P:(c + 1) * P],
                                               K[:, J, I, c, r * P:(r + 1) * P], ident[:, :])
                last.then_inc(wt_ready, 1)

            def transpose_k(b, s, c, first):
                I, J = STEPS[s]
                if (s, c) not in MIRROR_AT:
                    return
                g = MIRROR_AT[s, c]
                pe.wait_ge(k_up, b * SUMS + s * S + (c if I == J else S))
                if not first or g >= 2:
                    pe.wait_ge(k_low, b * MIRRORS + g - 1)
                for r in range(c if I == J else S):
                    last = nc.tensor.transpose(psM[:, g % 2, r * P:(r + 1) * P],
                                               K[:, I, J, r, c * P:(c + 1) * P], ident[:, :])
                last.then_inc(kt_ready, 1)

            def product(b, s, r):
                I, J = STEPS[s]
                if r == 0:
                    pe.wait_ge(xs_ready, b * S + J + 1)
                for rows, cols in ((I, J), (J, I))[:1 if I == J else 2]:
                    for h in range(2):
                        moving = K[:, rows, cols, r, :].rearrange("p (k h q) -> p k h q", h=2, q=P)[:, :, h, :]
                        into = acc[h * C:(h + 1) * C, cols * HALF:(cols + 1) * HALF]
                        last = nc.tensor.matmul(into.rearrange("p (k q) -> p k q", q=P), xs[:, rows * S + r, :],
                                                moving, start=(s in (0, 2) and rows == 0 and r == 0),
                                                stop=(s == NS - 1 and r == S - 1), skip_group_check=True)
                if r == S - 1:
                    last.then_inc(product_done, 1)

            def transpose_y(b):
                pe.wait_ge(yT_ready, 2 * (b + 1))
                for q in range(NT // 2):
                    last = nc.tensor.transpose(psY[:, q * P:(q + 1) * P], yT[:, q * P:(q + 1) * P], ident[:, :])
                last.then_inc(y_ready, 1)

            pe.wait_ge(u_in, 16)
            pe.wait_ge(ident_ready, 1)
            for t in range(NT):
                into = psY if t < NT // 2 else acc
                t0 = t % (NT // 2) * P
                last = nc.tensor.transpose(into[0:R, t0:t0 + P], Un[:, t, :], ident[:, :])
            last.then_inc(ut_ready, 1)
            pe.wait_ge(ut_copied, 2)
            for t in range(SUMS + LAG_K):
                if row := at_beat(t, 0):
                    outer(*row)
                    transpose_w(0, *row, True)
                if row := at_beat(t, LAG_K):
                    transpose_k(0, *row, True)
            with pe.Fori(1, B) as b:
                for t in range(BEATS):
                    if row := at_beat(t, LAG):
                        transpose_w(b, *row, False)
                    if row := at_beat(t, 0):
                        product(b - 1, *row)
                    if row := at_beat(t, LAG + LAG_K):
                        transpose_k(b, *row, False)
                    if t == SUMS + 1:
                        transpose_y(b - 1)
            for row in ROWS:
                product(B - 1, *row)
            transpose_y(B - 1)

        @block.vector
        def _(dve):
            def sum_row(b, s, r):
                I, J = STEPS[s]
                g, c0 = s * S + r, r * P if I == J else 0
                if r == 0:
                    dve.wait_ge(w_in[I][J], 16 * (b + 1))
                dve.wait_ge(wt_ready, b * SUMS + g + 1)
                row = K[:, I, J, r, c0:SQ]
                nc.vector.tensor_tensor(row, psT[:, g % 2, c0:SQ], row, ALU.add).then_inc(sum_done, 1)

            def times_a(b, s, r, first):
                I, J = STEPS[s]
                g, c0 = s * S + r, r * P if I == J else 0
                dve.wait_ge(sum_done, b * SUMS + g + 1)
                if first:
                    dve.wait_ge(a_ready, g + 1)
                row = K[:, I, J, r, c0:SQ]
                nc.vector.scalar_tensor_tensor(row, row, 1.0, A[:, A_AT[s, r]:A_AT[s, r] + SQ - c0], ALU.mult, ALU.mult,
                                               accum_out=part[:, I * S + r, J:J + 1]).then_inc(k_up, 1)

            def build(b, t, first):
                if row := at_beat(t, 0):
                    sum_row(b, *row)
                if row := at_beat(t, 1):
                    times_a(b, *row, first)

            def rsqrt(square, root_in, to, done, step, at):
                nc.vector.reciprocal(inv[:, :], root_in).then_inc(step, 1)
                dve.wait_ge(step, at + 1)
                nc.vector.tensor_tensor(nwt[:, :], inv[:, :], inv[:, :], ALU.mult).then_inc(step, 1)
                dve.wait_ge(step, at + 2)
                nc.vector.scalar_tensor_tensor(nwt[:, :], nwt[:, :], -0.5, square, ALU.mult, ALU.mult).then_inc(step, 1)
                dve.wait_ge(step, at + 3)
                nc.vector.scalar_tensor_tensor(to, nwt[:, :], 1.5, inv[:, :], ALU.add, ALU.mult).then_inc(done, 1)

            def scale_x(b):
                dve.wait_ge(k_up, (b + 1) * SUMS)
                dve.wait_ge(k_low, (b + 1) * MIRRORS)
                nc.vector.reduce_sum(deg2[:, :], part[:, :, :], AX.X).then_inc(deg_step, 1)
                dve.wait_ge(deg_step, 5 * b + 1)
                nc.vector.tensor_scalar(deg[:, :], deg2[:, :], 0.5, EPS_DEG, ALU.mult, ALU.max).then_inc(deg_ready, 1)
                dve.wait_ge(root_ready, b + 1)
                rsqrt(deg[:, :], root[:, :], d[:, :], deg_step, deg_step, 5 * b + 1)
                dve.wait_ge(deg_step, 5 * b + 5)
                dve.wait_ge(x_in, 16 * (b + 1))
                for I in range(S):
                    rows = xs[:, I * S:(I + 1) * S, :]
                    nc.vector.tensor_tensor(rows, rows, d[:, I * S:(I + 1) * S].unsqueeze(2).to_broadcast([P, S, C]),
                                            ALU.mult).then_inc(xs_ready, 1)

            def scale_y(b):
                nc.vector.tensor_scalar(dw[:, :], d[:, :], wsh[:, 0:1], None, ALU.mult).then_inc(dw_ready, 1)

            def residual(b):
                dve.wait_ge(y_ready, b + 1)
                dve.wait_ge(r_in, 16 * (b + 1))
                dve.wait_ge(dw_ready, b + 1)
                for t in range(NT):
                    last = nc.vector.scalar_tensor_tensor(z[:, t, :], psY[:, t * C:(t + 1) * C], dw[:, t:t + 1],
                                                          z[:, t, :], ALU.mult, ALU.add, accum_out=zsum[:, t:t + 1])
                last.then_inc(z_ready, 1)
                dve.wait_ge(z_ready, b + 1)
                nc.vector.tensor_scalar(nmean[:, :], zsum[:, :], -1.0 / C, None, ALU.mult).then_inc(nmean_ready, 1)

            def deviation(b):
                dve.wait_ge(zsq_ready, b + 1)
                nc.vector.tensor_scalar(var[:, :], zsq[:, :], 1.0 / C, EPS_LN, ALU.mult, ALU.add).then_inc(var_ready, 1)
                dve.wait_ge(std_ready, b + 1)
                rsqrt(var[:, :], zsum[:, :], rstd[:, :], rstd_ready, ln_step, 3 * b)

            nc.vector.memset(part[:, :, S:S + 1], 0.0).then_inc(part_zero, 1)
            dve.wait_ge(s_in, 16)
            nc.vector.tensor_scalar(wsh[:, :], wsc[:, :], 0.5, None, ALU.mult)
            dve.wait_ge(ut_ready, 1)
            for h, src in enumerate((psY, acc)):
                nc.vector.tensor_copy(UT[:, h * N // 2:(h + 1) * N // 2], src[0:R, :]).then_inc(ut_copied, 1)
            for t in range(SUMS + 1):
                build(0, t, True)
            scale_x(0)
            scale_y(0)
            with dve.Fori(1, B) as b:
                for t in range(SUMS + 1):
                    build(b, t, False)
                scale_x(b)
                residual(b - 1)
                scale_y(b)
                deviation(b - 1)
            residual(B - 1)
            deviation(B - 1)

        @block.scalar
        def _(act):
            def sigmoid(s, r):
                I, J = STEPS[s]
                g, n = s * S + r, SQ - r * P if I == J else SQ
                act.wait_ge(uu_ready, g + 1)
                nc.scalar.activation(A[:, A_AT[s, r]:A_AT[s, r] + n], psY[:, (g % 2) * SQ:(g % 2) * SQ + n],
                                     ACT.Sigmoid).then_inc(a_ready, 1)

            def mirror(b, s, c):
                I, J = STEPS[s]
                if (s, c) not in MIRROR_AT:
                    return
                g, n, at = MIRROR_AT[s, c], c * P if I == J else SQ, S if I == J else I
                act.wait_ge(kt_ready, b * MIRRORS + g + 1)
                nc.scalar.activation(K[:, J, I, c, 0:n], psM[:, g % 2, 0:n], ACT.Copy,
                                     accum_out=part[:, J * S + c, at:at + 1]).then_inc(k_low, 1)

            def drain_y(b):
                act.wait_ge(product_done, (b + 1) * NS)
                for h in range(2):
                    nc.scalar.copy(yT[:, h * SQ:(h + 1) * SQ], acc[:, h * SQ:(h + 1) * SQ]).then_inc(yT_ready, 1)

            def squares(b):
                act.wait_ge(centred, b + 1)
                for t in range(NT):
                    last = nc.scalar.activation(psY[:, t * C:(t + 1) * C], z[:, t, :], ACT.Square,
                                                accum_out=zsq[:, t:t + 1])
                last.then_inc(zsq_ready, 1)

            def root_of_deg(b):
                act.wait_ge(deg_ready, b + 1)
                nc.scalar.activation(root[:, :], deg[:, :], ACT.Sqrt).then_inc(root_ready, 1)

            def root_of_var(b):
                act.wait_ge(var_ready, b + 1)
                nc.scalar.activation(zsum[:, :], var[:, :], ACT.Sqrt).then_inc(std_ready, 1)

            act.wait_ge(part_zero, 1)
            for t in range(SUMS + LAG_K):
                if row := at_beat(t, 0):
                    sigmoid(*row)
                if row := at_beat(t, LAG_K):
                    mirror(0, *row)
            root_of_deg(0)
            with act.Fori(1, B) as b:
                for t in range(BEATS):
                    if t == SUMS:
                        drain_y(b - 1)
                    if row := at_beat(t, LAG + LAG_K):
                        mirror(b, *row)
                root_of_deg(b)
                squares(b - 1)
                root_of_var(b - 1)
            drain_y(B - 1)
            squares(B - 1)
            root_of_var(B - 1)

        @block.gpsimd
        def _(pool):
            def normalise(b):
                pool.wait_ge(z_ready, b + 1)
                pool.wait_ge(nmean_ready, b + 1)
                nc.gpsimd.tensor_tensor(z, z, nmean[:, :].unsqueeze(2).to_broadcast([P, NT, C]),
                                        ALU.add).then_inc(centred, 1)
                pool.wait_ge(centred, b + 1)
                pool.wait_ge(zsq_ready, b + 1)
                pool.wait_ge(rstd_ready, b + 1)
                nc.gpsimd.tensor_tensor(z, z, rstd[:, :].unsqueeze(2).to_broadcast([P, NT, C]),
                                        ALU.mult).then_inc(norm_done, 1)
                pool.wait_ge(norm_done, b + 1)
                pool.dma_start(out_v[b], z).then_inc(out_done, 16)

            nc.gpsimd.memset(ident[:, :], 0.0).then_inc(zeros, 1)
            pool.wait_ge(zeros, 1)
            nc.gpsimd.affine_select(out=ident[:, :], in_=ident[:, :], compare_op=ALU.not_equal, fill=1.0, base=0,
                                    pattern=[[-1, P]], channel_multiplier=1).then_inc(ident_ready, 1)
            pool.wait_ge(uu_ready, SUMS)
            pool.dma_start(z, x_v[0]).then_inc(r_in, 16)
            with pool.Fori(1, B) as b:
                normalise(b - 1)
                pool.wait_ge(out_done, 16 * b)
                pool.dma_start(z, x_v[b]).then_inc(r_in, 16)
            normalise(B - 1)
            pool.wait_ge(out_done, 16 * B)


_INS = ["x", "adj", "L0_gnn_U", "L0_gnn_w_scale"]
_OUT = ((8, 2048, 64), "float32")


def kernel(**inputs):
    import numpy as _np
    import concourse.bacc as _bacc
    from concourse import mybir as _mybir
    from concourse.bass_utils import run_bass_kernel_spmd as _run

    nc = _bacc.Bacc("TRN2", target_bir_lowering=False, num_devices=1)
    arrays, args = {}, []
    for name in _INS:
        a = _np.ascontiguousarray(inputs[name])
        arrays[f"in_{name}_dram"] = a
        args.append(nc.dram_tensor(f"in_{name}_dram", a.shape, _mybir.dt.from_np(a.dtype), kind="ExternalInput").ap())
    shape, dtype = _OUT
    args.append(nc.dram_tensor("out_dram", shape, _mybir.dt.from_np(_np.dtype(dtype)), kind="ExternalOutput").ap())
    graph_conv_norm(nc, *args)
    r = _run(nc, [arrays], core_ids=[0])
    return r.results[0]["out_dram"]
```

```python
import concourse.bass as bass
from concourse import mybir
from contextlib import ExitStack


def graph_conv_norm(nc: bass.Bass, x: bass.AP, adj: bass.AP, U: bass.AP, w_scale: bass.AP, out: bass.AP):
    fp32 = mybir.dt.float32
    bf16 = mybir.dt.bfloat16
    ALU = mybir.AluOpType
    ACT = mybir.ActivationFunctionType
    AX = mybir.AxisListType

    B, N, C = x.shape
    R = U.shape[1]
    P = 128
    NT = N // P
    S = 4
    SQ = S * P
    EPS_DEG = 1e-12
    EPS_LN = 1e-5

    STEPS = [(0, 0), (0, 1), (1, 1), (0, 2), (1, 2), (0, 3), (1, 3), (2, 2), (2, 3), (3, 3)]
    TURNS = [(I, m, r) for I, m in ((0, 0), (1, 0), (0, 1), (1, 1), (2, 0), (3, 0), (2, 1), (3, 1)) for r in range(S)]
    NTURNS = len(TURNS)
    LOW_DONE = TURNS.index((1, 1, S - 1))
    HALF_DONE = TURNS.index((3, 0, S - 1))
    NS = len(STEPS)
    ROWS = [(s, r) for s in range(NS) for r in range(S)]
    SUMS = len(ROWS)
    MIRROR_AT = {}
    for s, r in ROWS:
        if r or STEPS[s][0] != STEPS[s][1]:
            MIRROR_AT[s, r] = len(MIRROR_AT)
    MIRRORS = len(MIRROR_AT)

    EARLY = SUMS - 3 * S
    BUILD_AT, BUILD_RATE, FULL_RATE = 12.2, 0.75, 0.5
    LOAD_LAG = 5.5
    MIRROR_LAG = 7
    LATE_AT, LATE_RATE, LATE_LAG = -0.9, 0.9, 5
    LATE_MIRRORS = EARLY - 6
    Y_AT = 1.5
    OUTER_EVERY = 2
    LATE_SCALE_ROW = 1
    NORM_ROW = 8
    VAR_AT = NORM_ROW + 1
    PARTS = ((0, 1), (1, 2), (2, S))
    PART_ROWS = (S * STEPS.index((0, S - 1)) + S, S * STEPS.index((1, S - 1)) + S, SUMS)
    PART_MIRRORS = (MIRROR_AT[2, S - 1] + 1, MIRROR_AT[2, S - 1] + 1, MIRRORS)
    ROOT_AFTER = {18: 0, 24: 1}
    halves = (slice(0, NT // 2), slice(NT // 2, NT))

    OUTER_AT = {1 + OUTER_EVERY * (s - 1): s for s in range(1, NS)}

    NEEDS = [max(i for i, (rows, m, _) in enumerate(TURNS) if (rows, m) in ((I, J // 2), (J, I // 2)))
             for I, J in STEPS for r in range(S)]

    def plan(products, builds, late, norm):
        turns, late_end = [], 0
        if products:
            turns += [(g, 1, "product", -1, g) for g in range(NTURNS)]
            turns += [(HALF_DONE + 1.5, 3, "transpose_y", -1, 0)]
        if norm:
            turns += [(Y_AT, 3, "transpose_y", -2, 1)]
        if late:
            at = [LATE_AT + LATE_RATE * n for n in range(SUMS - EARLY + LATE_LAG)]
            turns += [(at[g - EARLY], 0, "build", -1, g) for g in range(EARLY, SUMS)]
            turns += [(at[max(0, g - EARLY + LATE_LAG)], 2, "mirror", -1, g) for g in range(LATE_MIRRORS, SUMS)]
            late_end = at[SUMS - 1 - EARLY + LATE_LAG]
        if builds:
            at = []
            for g in range(EARLY + MIRROR_LAG):
                at += [at[-1] + (BUILD_RATE if g < 3 * S else FULL_RATE) if at else 0]
                if products and g < EARLY:
                    at[g] = max(at[g], NEEDS[g] + LOAD_LAG, BUILD_AT, late_end if g >= LATE_SCALE_ROW + 2 else at[g])
            turns += [(at[g], 0, "build", 0, g) for g in range(EARLY)]
            turns += [(max(late_end, at[g + MIRROR_LAG]), 2, "mirror", 0, g) for g in range(LATE_MIRRORS)]
        turns = [turn for turn in sorted(turns) if turn[2] != "mirror" or ROWS[turn[4]] in MIRROR_AT]
        return [(kind, back, g) for *_, kind, back, g in turns]

    A_AT, a_cols = {}, 0
    for s, (I, J) in enumerate(STEPS):
        for r in range(S):
            A_AT[s, r] = a_cols
            a_cols += SQ - r * P if I == J else SQ

    adj_v = adj.rearrange("b (i r p) m -> b i p r m", r=S, p=P)
    x_v = x.rearrange("b (t p) c -> b p t c", p=P)
    out_v = out.rearrange("b (t p) c -> b p t c", p=P)
    U_v = U.rearrange("(t p) r -> p t r", p=P)

    ctx = ExitStack()
    with ctx:
        def sb(name, shape):
            return ctx.enter_context(nc.sbuf_tensor(name, shape, fp32))

        def sem(name):
            return ctx.enter_context(nc.semaphore(name))

        K = sb("K", [P, S, S // 2, S, 2, SQ])
        A = sb("A", [P, a_cols])
        work = sb("work", [P, 2 * NT * C])
        xs = work[:, 0:NT * C].rearrange("p (t c) -> p t c", c=C)
        z = work[:, NT * C:2 * NT * C].rearrange("p (t c) -> p t c", c=C)
        z_last = K[:, 0, 0, 0, :, :].rearrange("p j (t c) -> p (j t) c", c=C)

        G = P // R
        Un = A[:, a_cols - NT * R:a_cols].rearrange("p (t r) -> p t r", r=R)
        U_still = K[:, S - 1, 1, 0:2, :, :].rearrange("p a j (t g r) -> p (a j t) g r", g=G, r=R)
        U_moving = K[:, S - 1, 1, 2:4, :, :].rearrange("p a j (t g r) -> p (a j t) g r", g=G, r=R)
        U_low = K[:, S - 2, 1, 0:2, :, :].rearrange("p a j (t g r) -> p (a j t) g r", g=G, r=R)
        U_rest = K[:, S - 2, 1, 2, 0, 0:NT * R].rearrange("p (t r) -> p t r", r=R)
        Uh = K[:, S - 2, 1, 2, 1, 0:NT * R // 2].bitcast(bf16).rearrange("p (t r) -> p t r", r=R)
        Um = K[:, S - 2, 1, 3, 0, 0:NT * R // 2].bitcast(bf16).rearrange("p (t r) -> p t r", r=R)
        UT_still = work[:, 0:N // 2].bitcast(bf16)
        UT_moving = work[:, N // 2:N].bitcast(bf16)
        UT_low = A[:, a_cols - N // 2:a_cols].bitcast(bf16)
        yT = sb("yT", [P, SQ])
        ident = sb("ident", [P, P])
        part = sb("part", [P, NT, S + 1])
        deg2 = sb("deg2", [P, NT])
        deg = sb("deg", [P, NT])
        root = sb("root", [P, NT])
        inv = sb("inv", [P, NT])
        nwt = sb("nwt", [P, NT])
        d = sb("d", [P, NT])
        dw = sb("dw", [P, NT])
        wsc = sb("wsc", [P, 1])
        wsh = sb("wsh", [P, 1])
        zsum = sb("zsum", [P, NT])
        nmean = sb("nmean", [P, NT])
        zsq = sb("zsq", [P, NT])
        var = sb("var", [P, NT])
        rstd = sb("rstd", [P, NT])

        acc = ctx.enter_context(nc.psum_tensor("acc", [P, 2 * SQ], fp32))
        psT = ctx.enter_context(nc.psum_tensor("psT", [P, 2, SQ], fp32))
        psM = ctx.enter_context(nc.psum_tensor("psM", [P, 2, SQ], fp32))
        psY = ctx.enter_context(nc.psum_tensor("psY", [P, NT * C], fp32))

        def square(I, J, r, c0, c1):
            return K[:, I, J // 2, r, J % 2, c0:c1]

        psT_flat = psT[:, :, :].rearrange("p a b -> p (a b)")
        psM_flat = psM[:, :, :].rearrange("p a b -> p (a b)")
        outer_bank = [psY[:, 0:SQ], psY[:, SQ:2 * SQ], acc[:, 0:SQ], acc[:, SQ:2 * SQ]]

        w_in = [[[sem(f"w_in_{I}{m}{r}") for r in range(S)] for m in range(S // 2)] for I in range(S)]
        u_in = sem("u_in")
        s_in = sem("s_in")
        x_in = [sem("x_in_low"), sem("x_in_high")]
        r_in = sem("r_in")
        out_done = sem("out_done")
        zeros = sem("zeros")
        ident_ready = sem("ident_ready")
        part_zero = sem("part_zero")
        u_split = sem("u_split")
        still_spread = sem("still_spread")
        moving_spread = sem("moving_spread")
        low_spread = sem("low_spread")
        ut_ready = sem("ut_ready")
        still_copied = sem("still_copied")
        moving_copied = sem("moving_copied")
        low_copied = sem("low_copied")
        uu_ready = sem("uu_ready")
        a_ready = sem("a_ready")
        wt_ready = sem("wt_ready")
        sum_done = sem("sum_done")
        k_up = sem("k_up")
        kt_ready = sem("kt_ready")
        k_low = sem("k_low")
        deg_step = sem("deg_step")
        deg_ready = sem("deg_ready")
        root_ready = sem("root_ready")
        xs_ready = sem("xs_ready")
        dw_ready = sem("dw_ready")
        product_done = sem("product_done")
        yT_ready = sem("yT_ready")
        y_ready = sem("y_ready")
        z_ready = sem("z_ready")
        nmean_ready = sem("nmean_ready")
        centred = sem("centred")
        zsq_ready = sem("zsq_ready")
        var_ready = sem("var_ready")
        std_ready = sem("std_ready")
        ln_step = sem("ln_step")
        rstd_ready = sem("rstd_ready")
        norm_done = sem("norm_done")
        last_in = sem("last_in")
        last_done = sem("last_done")
        last_out = sem("last_out")

        block = ctx.enter_context(nc.Block())

        @block.sync
        def _(sp):
            def load(b, first):
                for n in range(0, NTURNS, S):
                    if first and n + 2 * S == NTURNS:
                        sp.wait_ge(ut_ready, 3)
                    for r in (1, 0, 2, 3):
                        if not first and r:
                            sp.wait_ge(product_done, (b - 1) * NTURNS + n + r + 1)
                        I, m, _ = TURNS[n]
                        sp.dma_start(K[:, I, m, r, :, :].rearrange("p j q -> p (j q)"),
                                     adj_v[b, I, :, r, 2 * m * SQ:2 * (m + 1) * SQ]).then_inc(w_in[I][m][r], 16)

            sp.dma_start(Un, U_v).then_inc(u_in, 16)
            sp.dma_start(wsc[:, :], w_scale.partition_broadcast(P)).then_inc(s_in, 16)
            load(0, True)
            sp.wait_ge(uu_ready, SUMS)
            for h in range(2):
                sp.dma_start(xs[:, halves[h], :], x_v[0, :, halves[h], :]).then_inc(x_in[h], 16)
            with sp.Fori(1, B) as b:
                load(b, False)
            sp.wait_ge(product_done, (B - 1) * NTURNS + 1)
            sp.dma_start(z_last, x_v[B - 1]).then_inc(last_in, 16)
            for h in range(2):
                sp.wait_ge(last_done, h + 1)
                sp.dma_start(out_v[B - 1, :, halves[h], :], z_last[:, halves[h], :]).then_inc(last_out, 16)
            sp.wait_ge(last_out, 2 * 16)

        @block.tensor
        def _(pe):
            def outer(s):
                I, J = STEPS[s]
                for r in range(S):
                    c0 = r * P if I == J else 0
                    if s:
                        pe.wait_ge(a_ready, (s - 1) * S + r + 1)
                    rows, cols = slice((I * S + r) * P, (I * S + r + 1) * P), slice(J * SQ + c0, (J + 1) * SQ)
                    nc.tensor.matmul(outer_bank[r][:, 0:SQ - c0], UT_still[:, rows], UT_moving[:, cols],
                                     start=True, stop=False)
                    nc.tensor.matmul(outer_bank[r][:, 0:SQ - c0], UT_low[:, rows], UT_low[:, cols],
                                     start=False, stop=True).then_inc(uu_ready, 1)

            def transpose_w(b, s, r, first):
                I, J = STEPS[s]
                g = s * S + r
                if r == 0:
                    for c in range(S):
                        pe.wait_ge(w_in[J][I // 2][c], 16 * (b + 1))
                if not first or g >= 2:
                    pe.wait_ge(sum_done, b * SUMS + g - 1)
                for c in range(r if I == J else 0, S):
                    last = nc.tensor.transpose(psT[:, g % 2, c * P:(c + 1) * P],
                                               square(J, I, c, r * P, (r + 1) * P), ident[:, :])
                last.then_inc(wt_ready, 1)

            def transpose_k(b, s, c, first):
                I, J = STEPS[s]
                g = MIRROR_AT[s, c]
                pe.wait_ge(k_up, b * SUMS + s * S + (c if I == J else S))
                if not first or g >= 2:
                    pe.wait_ge(k_low, b * MIRRORS + g - 1)
                for r in range(c if I == J else S):
                    last = nc.tensor.transpose(psM[:, g % 2, r * P:(r + 1) * P],
                                               square(I, J, r, c * P, (c + 1) * P), ident[:, :])
                last.then_inc(kt_ready, 1)

            def product(b, I, m, r):
                if r == 0:
                    pe.wait_ge(xs_ready, b * S + I + 1)
                for h in range(2):
                    last = nc.tensor.matmul(acc[h * C:(h + 1) * C, m * SQ:(m + 1) * SQ], xs[:, I * S + r, :],
                                            K[:, I, m, r, h, :], start=(I == 0 and r == 0),
                                            stop=(I == S - 1 and r == S - 1), skip_group_check=True)
                last.then_inc(product_done, 1)

            def transpose_y(b, h):
                pe.wait_ge(yT_ready, 2 * b + h + 1)
                for q in range(S):
                    last = nc.tensor.transpose(psY[:, h * SQ + q * P:h * SQ + (q + 1) * P],
                                               yT[:, q * P:(q + 1) * P], ident[:, :])
                last.then_inc(y_ready, 1)

            def run_pass(b, first, products, builds, late, norm):
                for kind, back, g in plan(products, builds, late, norm):
                    if kind == "product":
                        product(b + back, *TURNS[g])
                    elif kind == "transpose_y":
                        transpose_y(b + back, g)
                    elif kind == "mirror":
                        transpose_k(b + back, *ROWS[g], first)
                    else:
                        transpose_w(b + back, *ROWS[g], first)
                        if first and g in OUTER_AT:
                            outer(OUTER_AT[g])

            def transpose_u(parts, banks):
                for t in range(NT):
                    t0 = t % (NT // 2) * P
                    last = nc.tensor.transpose(banks[t * 2 // NT][:, t0:t0 + P],
                                               parts[:, t, :, :].rearrange("p g r -> p (g r)"), ident[:, :])
                last.then_inc(ut_ready, 1)

            pe.wait_ge(ident_ready, 1)
            pe.wait_ge(still_spread, 3)
            transpose_u(U_still, (psY, acc))
            pe.wait_ge(moving_spread, 1)
            transpose_u(U_moving, (psT_flat, psM_flat))
            pe.wait_ge(u_split, 4)
            pe.wait_ge(low_spread, 1)
            pe.wait_ge(still_copied, 2)
            transpose_u(U_low, (psY, acc))
            pe.wait_ge(moving_copied, 2)
            pe.wait_ge(low_copied, 2)
            outer(0)
            run_pass(0, True, False, True, False, False)
            run_pass(1, False, True, True, True, False)
            with pe.Fori(2, B) as b:
                run_pass(b, False, True, True, True, True)
            run_pass(B, False, True, False, True, True)
            transpose_y(B - 1, 1)

        @block.vector
        def _(dve):
            def y_tile(t):
                at = t // (2 * S) * 2 * S + t % S * 2 + t // S % 2
                return psY[:, at * C:(at + 1) * C]

            def sum_row(b, s, r):
                I, J = STEPS[s]
                g, c0 = s * S + r, r * P if I == J else 0
                dve.wait_ge(w_in[I][J // 2][r], 16 * (b + 1))
                dve.wait_ge(wt_ready, b * SUMS + g + 1)
                row = square(I, J, r, c0, SQ)
                nc.vector.tensor_tensor(row, psT[:, g % 2, c0:SQ], row, ALU.add).then_inc(sum_done, 1)

            def times_a(b, s, r, first):
                I, J = STEPS[s]
                g, c0 = s * S + r, r * P if I == J else 0
                dve.wait_ge(sum_done, b * SUMS + g + 1)
                if first:
                    dve.wait_ge(a_ready, g + 1)
                row = square(I, J, r, c0, SQ)
                nc.vector.scalar_tensor_tensor(row, row, 1.0, A[:, A_AT[s, r]:A_AT[s, r] + SQ - c0], ALU.mult, ALU.mult,
                                               accum_out=part[:, I * S + r, J:J + 1]).then_inc(k_up, 1)

            def rsqrt_step(k, square, root_in, to, cols, done, step, at):
                r, n = inv[:, cols], nwt[:, cols]
                if k == 0:
                    nc.vector.reciprocal(r, root_in).then_inc(step, 1)
                elif k == 1:
                    dve.wait_ge(step, at + 1)
                    nc.vector.tensor_tensor(n, r, r, ALU.mult).then_inc(step, 1)
                elif k == 2:
                    dve.wait_ge(step, at + 2)
                    nc.vector.scalar_tensor_tensor(n, n, -0.5, square, ALU.mult, ALU.mult).then_inc(step, 1)
                elif k == 3:
                    dve.wait_ge(step, at + 3)
                    nc.vector.scalar_tensor_tensor(to, n, 1.5, r, ALU.add, ALU.mult).then_inc(done, 1)

            def scale_step(b, piece, k):
                I0, I1 = PARTS[piece]
                cols, at = slice(I0 * S, I1 * S), 5 * (len(PARTS) * b + piece)
                if k == 0:
                    dve.wait_ge(k_up, b * SUMS + PART_ROWS[piece])
                    dve.wait_ge(k_low, b * MIRRORS + PART_MIRRORS[piece])
                    nc.vector.reduce_sum(deg2[:, cols], part[:, cols, :], AX.X).then_inc(deg_step, 1)
                elif k == 1:
                    dve.wait_ge(deg_step, at + 1)
                    nc.vector.tensor_scalar(deg[:, cols], deg2[:, cols], 0.5, EPS_DEG, ALU.mult,
                                            ALU.max).then_inc(deg_ready, 1)
                else:
                    if k == 2:
                        dve.wait_ge(root_ready, len(PARTS) * b + piece + 1)
                    rsqrt_step(k - 2, deg[:, cols], root[:, cols], d[:, cols], cols, deg_step, deg_step, at + 1)

            def scale_x(b, piece):
                I0, I1 = PARTS[piece]
                dve.wait_ge(deg_step, 5 * (len(PARTS) * b + piece) + 5)
                dve.wait_ge(x_in[I0 * 2 // S], 16 * (b + 1))
                for I in range(I0, I1):
                    rows = xs[:, I * S:(I + 1) * S, :]
                    nc.vector.tensor_tensor(rows, rows, d[:, I * S:(I + 1) * S].unsqueeze(2).to_broadcast([P, S, C]),
                                            ALU.mult).then_inc(xs_ready, 1)

            def scale_y(b):
                nc.vector.tensor_scalar(dw[:, :], d[:, :], wsh[:, 0:1], None, ALU.mult).then_inc(dw_ready, 1)

            def residual_tile(z, t):
                return nc.vector.scalar_tensor_tensor(z[:, t, :], y_tile(t), dw[:, t:t + 1], z[:, t, :],
                                                      ALU.mult, ALU.add, accum_out=zsum[:, t:t + 1])

            def residual(b):
                dve.wait_ge(y_ready, 2 * (b + 1))
                dve.wait_ge(r_in, 16 * (b + 1))
                dve.wait_ge(dw_ready, b + 1)
                for t in range(NT):
                    last = residual_tile(z, t)
                last.then_inc(z_ready, 1)
                dve.wait_ge(z_ready, b + 1)
                nc.vector.tensor_scalar(nmean[:, :], zsum[:, :], -1.0 / C, None, ALU.mult).then_inc(nmean_ready, 1)

            def finish(h):
                cols, n = halves[h], B - 1 + h
                dve.wait_ge(y_ready, 2 * (B - 1) + h + 1)
                if h == 0:
                    dve.wait_ge(last_in, 16)
                    dve.wait_ge(dw_ready, B)
                for t in range(NT // 2 * h, NT // 2 * (h + 1)):
                    last = residual_tile(z_last, t)
                last.then_inc(z_ready, 1)
                dve.wait_ge(z_ready, n + 1)
                nc.vector.tensor_scalar(nmean[:, cols], zsum[:, cols], -1.0 / C, None,
                                        ALU.mult).then_inc(nmean_ready, 1)
                dve.wait_ge(zsq_ready, n + 1)
                nc.vector.tensor_scalar(var[:, cols], zsq[:, cols], 1.0 / C, EPS_LN, ALU.mult,
                                        ALU.add).then_inc(var_ready, 1)
                dve.wait_ge(std_ready, n + 1)
                dve.wait_ge(norm_done, B - 1)
                for k in range(4):
                    rsqrt_step(k, var[:, cols], zsum[:, cols], rstd[:, cols], cols, rstd_ready, ln_step, 3 * n)
                dve.wait_ge(rstd_ready, n + 1)
                for t in range(NT // 2 * h, NT // 2 * (h + 1)):
                    last = nc.vector.tensor_scalar(z_last[:, t, :], z_last[:, t, :], nmean[:, t:t + 1],
                                                   rstd[:, t:t + 1], ALU.add, ALU.mult)
                last.then_inc(last_done, 1)

            def deviation_step(b, k):
                if k == 0:
                    dve.wait_ge(zsq_ready, b + 1)
                    nc.vector.tensor_scalar(var[:, :], zsq[:, :], 1.0 / C, EPS_LN, ALU.mult,
                                            ALU.add).then_inc(var_ready, 1)
                else:
                    if k == 1:
                        dve.wait_ge(std_ready, b + 1)
                    rsqrt_step(k - 1, var[:, :], zsum[:, :], rstd[:, :], slice(0, NT), rstd_ready, ln_step, 3 * b)

            def build_rows(b, g0, g1, first, late, norm):
                for g in range(g0, g1 + 1):
                    if g < g1:
                        sum_row(b, *ROWS[g])
                    scales = [(g - PART_ROWS[0], b, 0), (g - PART_ROWS[1], b, 1)] if g < g1 else []
                    if late:
                        scales += [(g - LATE_SCALE_ROW, b - 1, 2)]
                    for n, of, piece in scales:
                        if 2 <= n < 4:
                            scale_step(of, piece, 2 * n - 2)
                    if g > g0:
                        times_a(b, *ROWS[g - 1], first)
                    for n, of, piece in scales:
                        if 0 <= n < 4:
                            scale_step(of, piece, max(n, 2 * n - 1))
                        if n == 3:
                            scale_x(of, piece)
                    if late and g == LATE_SCALE_ROW + 3:
                        scale_y(b - 1)
                    if norm and NORM_ROW <= g < NORM_ROW + 5:
                        deviation_step(b - 2, g - NORM_ROW)

            def run_pass(b, first, late, norm):
                if late:
                    build_rows(b - 1, EARLY, SUMS, False, False, False)
                if norm:
                    residual(b - 2)
                build_rows(b, 0, EARLY, first, late, norm)

            def spread(groups, of):
                return of.unsqueeze(2).to_broadcast([P, NT, groups, R])

            nc.vector.memset(part[:, :, S:S + 1], 0.0).then_inc(part_zero, 1)
            dve.wait_ge(u_in, 16)
            nc.vector.tensor_copy(Uh, Un).then_inc(u_split, 1)
            dve.wait_ge(u_split, 1)
            nc.vector.tensor_copy(U_still[:, :, 0:3, :], spread(3, Uh)).then_inc(still_spread, 1)
            dve.wait_ge(still_spread, 1)
            nc.vector.tensor_tensor(U_rest, Un, U_still[:, :, 0, :], ALU.subtract).then_inc(u_split, 1)
            dve.wait_ge(u_split, 2)
            nc.vector.tensor_copy(Um, U_rest).then_inc(u_split, 1)
            dve.wait_ge(u_split, 3)
            nc.vector.tensor_copy(U_still[:, :, 3:6, :], spread(3, Um)).then_inc(still_spread, 1)
            dve.wait_ge(still_spread, 2)
            nc.vector.tensor_tensor(U_low[:, :, 0, :], U_rest, U_still[:, :, 3, :], ALU.subtract).then_inc(u_split, 1)
            dve.wait_ge(u_split, 4)
            nc.vector.tensor_copy(U_still[:, :, 6:8, :], spread(2, U_low[:, :, 0, :])).then_inc(still_spread, 1)
            dve.wait_ge(s_in, 16)
            nc.vector.tensor_scalar(wsh[:, :], wsc[:, :], 0.5, None, ALU.mult)
            dve.wait_ge(ut_ready, 1)
            for h, bank in enumerate((psY, acc)):
                nc.vector.tensor_copy(UT_still[:, h * N // 2:(h + 1) * N // 2], bank[:, :]).then_inc(still_copied, 1)
            dve.wait_ge(ut_ready, 3)
            nc.vector.tensor_copy(UT_low[:, 0:N // 2], psY[:, :]).then_inc(low_copied, 1)
            run_pass(0, True, False, False)
            dve.wait_ge(a_ready, SUMS)
            run_pass(1, False, True, False)
            with dve.Fori(2, B) as b:
                run_pass(b, False, True, True)
            build_rows(B - 1, EARLY, SUMS, False, False, False)
            residual(B - 2)
            for k in range(6):
                scale_step(B - 1, 2, k)
            scale_x(B - 1, 2)
            scale_y(B - 1)
            for k in range(5):
                deviation_step(B - 2, k)
            for h in range(2):
                finish(h)

        @block.scalar
        def _(act):
            def sigmoid(s, r):
                I, J = STEPS[s]
                g, n = s * S + r, SQ - r * P if I == J else SQ
                act.wait_ge(uu_ready, SUMS if s == NS - 1 else g + 1)
                nc.scalar.activation(A[:, A_AT[s, r]:A_AT[s, r] + n], outer_bank[r][:, 0:n],
                                     ACT.Sigmoid).then_inc(a_ready, 1)

            def mirror(b, s, c):
                I, J = STEPS[s]
                g, n, at = MIRROR_AT[s, c], c * P if I == J else SQ, S if I == J else I
                act.wait_ge(kt_ready, b * MIRRORS + g + 1)
                nc.scalar.activation(square(J, I, c, 0, n), psM[:, g % 2, 0:n], ACT.Copy,
                                     accum_out=part[:, J * S + c, at:at + 1]).then_inc(k_low, 1)

            def drain_y(b, h):
                act.wait_ge(product_done, b * NTURNS + (NTURNS if h else HALF_DONE + 1))
                if h:
                    act.wait_ge(y_ready, 2 * b + 1)
                nc.scalar.copy(yT[:, :], acc[:, h * SQ:(h + 1) * SQ]).then_inc(yT_ready, 1)

            def squares(b):
                act.wait_ge(centred, b + 1)
                for t in range(NT):
                    last = nc.scalar.activation(psY[:, t * C:(t + 1) * C], z[:, t, :], ACT.Square,
                                                accum_out=zsq[:, t:t + 1])
                last.then_inc(zsq_ready, 1)

            def root_of_deg(b, piece):
                I0, I1 = PARTS[piece]
                cols = slice(I0 * S, I1 * S)
                act.wait_ge(deg_ready, len(PARTS) * b + piece + 1)
                nc.scalar.activation(root[:, cols], deg[:, cols], ACT.Sqrt).then_inc(root_ready, 1)

            def root_of_var(b):
                act.wait_ge(var_ready, b + 1)
                nc.scalar.activation(zsum[:, :], var[:, :], ACT.Sqrt).then_inc(std_ready, 1)

            def finish(h):
                cols, n = halves[h], B - 1 + h
                act.wait_ge(nmean_ready, n + 1)
                for t in range(NT // 2 * h, NT // 2 * (h + 1)):
                    last = nc.scalar.activation(psY[:, t * C:(t + 1) * C], z_last[:, t, :], ACT.Square,
                                                bias=nmean[:, t:t + 1], accum_out=zsq[:, t:t + 1])
                last.then_inc(zsq_ready, 1)
                act.wait_ge(var_ready, n + 1)
                nc.scalar.activation(zsum[:, cols], var[:, cols], ACT.Sqrt).then_inc(std_ready, 1)

            def run_pass(b, first, products, builds, late, norm):
                for kind, back, g in plan(products, builds, late, norm):
                    if kind == "transpose_y" and back == -1 and not builds:
                        finish(0)
                    elif kind == "mirror":
                        mirror(b + back, *ROWS[g])
                        if g in ROOT_AFTER:
                            root_of_deg(b + back, ROOT_AFTER[g])
                        if back and g == SUMS - 1:
                            root_of_deg(b - 1, 2)
                            if norm:
                                squares(b - 2)
                                if not builds:
                                    root_of_var(b - 2)
                    elif kind == "build" and g == VAR_AT and not back and norm:
                        root_of_var(b - 2)
                    elif kind == "product" and g == HALF_DONE:
                        drain_y(b - 1, 0)
                    elif kind == "product" and g in (LOW_DONE, NTURNS - 1):
                        h = int(g > LOW_DONE)
                        if builds:
                            act.wait_ge(product_done, (b - 1) * NTURNS + g + 1)
                            act.dma_start(xs[:, halves[h], :], x_v[b, :, halves[h], :]).then_inc(x_in[h], 16)
                        if h:
                            drain_y(b - 1, 1)
                    elif kind == "build" and first and g in OUTER_AT:
                        for r in range(S):
                            sigmoid(OUTER_AT[g], r)

            for g, steps, of in ((0, 1, Uh), (1, 3, Um), (2, 4, U_low[:, :, 0, :])):
                act.wait_ge(u_split, steps)
                groups = U_moving[:, :, g:G:3, :]
                last = nc.scalar.copy(groups, of.unsqueeze(2).to_broadcast([P, NT, (G - g + 2) // 3, R]))
            last.then_inc(moving_spread, 1)
            act.wait_ge(ut_ready, 2)
            for h, bank in enumerate((psT_flat, psM_flat)):
                nc.scalar.copy(UT_moving[:, h * N // 2:(h + 1) * N // 2], bank).then_inc(moving_copied, 1)
            act.wait_ge(ut_ready, 3)
            nc.scalar.copy(UT_low[:, N // 2:N], acc[:, :]).then_inc(low_copied, 1)
            act.wait_ge(part_zero, 1)
            for r in range(S):
                sigmoid(0, r)
            run_pass(0, True, False, True, False, False)
            run_pass(1, False, True, True, True, False)
            with act.Fori(2, B) as b:
                run_pass(b, False, True, True, True, True)
            run_pass(B, False, True, False, True, True)
            finish(1)

        @block.gpsimd
        def _(pool):
            def normalise(b):
                pool.wait_ge(z_ready, b + 1)
                pool.wait_ge(nmean_ready, b + 1)
                nc.gpsimd.tensor_tensor(z, z, nmean[:, :].unsqueeze(2).to_broadcast([P, NT, C]),
                                        ALU.add).then_inc(centred, 1)
                pool.wait_ge(centred, b + 1)
                pool.wait_ge(zsq_ready, b + 1)
                pool.wait_ge(rstd_ready, b + 1)
                nc.gpsimd.tensor_tensor(z, z, rstd[:, :].unsqueeze(2).to_broadcast([P, NT, C]),
                                        ALU.mult).then_inc(norm_done, 1)
                pool.wait_ge(norm_done, b + 1)

            nc.gpsimd.memset(ident[:, :], 0.0).then_inc(zeros, 1)
            pool.wait_ge(zeros, 1)
            nc.gpsimd.affine_select(out=ident[:, :], in_=ident[:, :], compare_op=ALU.not_equal, fill=1.0, base=0,
                                    pattern=[[-1, P]], channel_multiplier=1).then_inc(ident_ready, 1)
            nc.gpsimd.memset(U_low[:, :, 1:G, :], 0.0).then_inc(low_spread, 1)
            pool.wait_ge(uu_ready, SUMS)
            pool.dma_start(z, x_v[0]).then_inc(r_in, 16)
            with pool.Fori(0, B - 2) as b:
                normalise(b)
                pool.dma_start(out_v[b], z).then_inc(out_done, 16)
                pool.wait_ge(out_done, 16 * (b + 1))
                pool.dma_start(z, x_v[b + 1]).then_inc(r_in, 16)
            normalise(B - 2)
            pool.dma_start(out_v[B - 2], z).then_inc(out_done, 16)
            pool.wait_ge(out_done, 16 * (B - 1))


_INS = ["x", "adj", "L0_gnn_U", "L0_gnn_w_scale"]
_OUT = ((8, 2048, 64), "float32")


def kernel(**inputs):
    import numpy as _np
    import concourse.bacc as _bacc
    from concourse import mybir as _mybir
    from concourse.bass_utils import run_bass_kernel_spmd as _run

    nc = _bacc.Bacc("TRN2", target_bir_lowering=False, num_devices=1)
    arrays, args = {}, []
    for name in _INS:
        a = _np.ascontiguousarray(inputs[name])
        arrays[f"in_{name}_dram"] = a
        args.append(nc.dram_tensor(f"in_{name}_dram", a.shape, _mybir.dt.from_np(a.dtype), kind="ExternalInput").ap())
    shape, dtype = _OUT
    args.append(nc.dram_tensor("out_dram", shape, _mybir.dt.from_np(_np.dtype(dtype)), kind="ExternalOutput").ap())
    graph_conv_norm(nc, *args)
    r = _run(nc, [arrays], core_ids=[0])
    return r.results[0]["out_dram"]
```
